# Optimizing a Trainium2 kernel written in Bass

```python
import numpy as np
import jax
import jax.numpy as jnp

def _softmax(x, axis=-1):
    return jax.nn.softmax(x, axis=axis)

def _gelu(x):
    return jax.nn.gelu(x, approximate=True)

def _silu(x):
    return jax.nn.silu(x)

def _sigmoid(x):
    return jax.nn.sigmoid(x)

def _layernorm(x, axis=-1, eps=1e-05):
    m = jnp.mean(x, axis=axis, keepdims=True)
    v = jnp.var(x, axis=axis, keepdims=True)
    return (x - m) / jnp.sqrt(v + eps)

def _scatter_add(tgt, idx, src, axis=0):
    return tgt.at[idx].add(src)

def _segment_sum(src, seg, n):
    return jax.ops.segment_sum(src, seg, n)
kernel_name = 'mk_adj_resnorm_d1_adj_r2_c26ffe'

def setup_inputs(seed: int=0):
    np.random.seed(seed)
    _w = jnp.asarray

    def _rec_inputs():
        import jax
        import jax.numpy as jnp
        _gk = jax.random.key(seed)
        x = 7.22e-05 + 1 * jax.random.normal(jax.random.fold_in(_gk, 1), (128, 64, 512), jnp.float32)
        _a = jax.random.bernoulli(jax.random.fold_in(_gk, 2), 0.125, (128, 64, 64))
        _a = jnp.logical_or(_a, jnp.eye(64, dtype=bool))
        adj = _a.astype(jnp.int32)
        return (x, adj)
    x, adj = _rec_inputs()

    def _L0_gnn_setup():
        import jax, jax.numpy as jnp
        import numpy as np
        import math
        D_MODEL = 512
        N_HEADS = 16
        D_HEAD = D_MODEL // N_HEADS
        B, S = (4, 1024)
        key = jax.random.key(seed)
        ks = jax.random.split(key, 10)
        x = jax.random.normal(ks[0], (B, S, D_MODEL), dtype=jnp.float32)
        mask = jax.random.randint(ks[1], (B, S, S), 0, 2, dtype=jnp.int32)
        eye = jnp.eye(S, dtype=jnp.int32)[None]
        mask = jnp.maximum(mask, eye)
        std = 1.0 / math.sqrt(D_MODEL)
        Wq = jax.random.normal(ks[2], (D_MODEL, D_MODEL), dtype=jnp.float32) * std
        Wk = jax.random.normal(ks[3], (D_MODEL, D_MODEL), dtype=jnp.float32) * std
        Wv = jax.random.normal(ks[4], (D_MODEL, D_MODEL), dtype=jnp.float32) * std
        Wo = jax.random.normal(ks[5], (D_MODEL, D_MODEL), dtype=jnp.float32) * std
        bq = jnp.zeros((D_MODEL,), dtype=jnp.float32)
        bk = jnp.zeros((D_MODEL,), dtype=jnp.float32)
        bv = jnp.zeros((D_MODEL,), dtype=jnp.float32)
        bo = jnp.zeros((D_MODEL,), dtype=jnp.float32)
        return {'x': x, 'mask': mask, 'Wq': Wq, 'bq': bq, 'Wk': Wk, 'bk': bk, 'Wv': Wv, 'bv': bv, 'Wo': Wo, 'bo': bo}
    _L0_gnn_all = _L0_gnn_setup()
    _L0_gnn_in = {k: v for k, v in _L0_gnn_all.items() if k in ('Wq', 'bq', 'Wk', 'bk', 'Wv', 'bv', 'Wo', 'bo')}
    del _L0_gnn_all
    return {'x': x, 'adj': adj, 'L0_gnn_Wq': _L0_gnn_in['Wq'], 'L0_gnn_bq': _L0_gnn_in['bq'], 'L0_gnn_Wk': _L0_gnn_in['Wk'], 'L0_gnn_bk': _L0_gnn_in['bk'], 'L0_gnn_Wv': _L0_gnn_in['Wv'], 'L0_gnn_bv': _L0_gnn_in['bv'], 'L0_gnn_Wo': _L0_gnn_in['Wo'], 'L0_gnn_bo': _L0_gnn_in['bo']}

def reference(x, adj, L0_gnn_Wq, L0_gnn_bq, L0_gnn_Wk, L0_gnn_bk, L0_gnn_Wv, L0_gnn_bv, L0_gnn_Wo, L0_gnn_bo):
    import jax
    import jax.numpy as jnp

    def _L0_gnn_ref(x, mask, Wq, bq, Wk, bk, Wv, bv, Wo, bo):
        import jax, jax.numpy as jnp
        import numpy as np
        import math
        D_MODEL = 512
        N_HEADS = 16
        D_HEAD = D_MODEL // N_HEADS
        B, S = (4, 1024)
        b, s, _ = x.shape
        scale = 1.0 / math.sqrt(D_HEAD)

        def heads(t):
            return t.reshape(b, s, N_HEADS, D_HEAD).transpose(0, 2, 1, 3)
        q = heads(x @ Wq + bq)
        k = heads(x @ Wk + bk)
        v = heads(x @ Wv + bv)
        scores = jnp.einsum('bhqd,bhkd->bhqk', q, k) * scale
        scores = jnp.where(mask[:, None] == 0, -jnp.inf, scores)
        attn = jax.nn.softmax(scores, axis=-1)
        out = jnp.einsum('bhqk,bhkd->bhqd', attn, v)
        out = out.transpose(0, 2, 1, 3).reshape(b, s, D_MODEL)
        return out @ Wo + bo
    x = _layernorm(x + _L0_gnn_ref(x, adj, L0_gnn_Wq, L0_gnn_bq, L0_gnn_Wk, L0_gnn_bk, L0_gnn_Wv, L0_gnn_bv, L0_gnn_Wo, L0_gnn_bo), axis=-1)
    return x

_drawn_inputs = setup_inputs


def setup_inputs(seed=0):
    import zlib

    import numpy as np

    out = dict(_drawn_inputs(seed))
    spreads = {'L0_gnn_bq': (0.0, 0.1),
     'L0_gnn_bk': (0.0, 0.1),
     'L0_gnn_bv': (0.0, 0.1),
     'L0_gnn_bo': (0.0, 0.1)}
    factors = {}
    for name, (base, spread) in spreads.items():
        noise = np.random.default_rng([zlib.crc32(name.encode()), seed]).standard_normal(out[name].shape)
        drawn = base * np.exp(spread * noise) if base else spread * noise
        out[name] = jnp.asarray(drawn.astype(out[name].dtype))
    for name, factor in factors.items():
        out[name] = (out[name] * factor).astype(out[name].dtype)
    return out
```

```python
from contextlib import ExitStack

import concourse.bass as bass
from concourse import mybir

F32 = mybir.dt.float32
F32R = mybir.dt.float32r
I32 = mybir.dt.int32
ALU = mybir.AluOpType
ACT = mybir.ActivationFunctionType
AX_X = mybir.AxisListType.X

P = 128
GRAPHS, NODES, D = 128, 64, 512
HEADS = 16
DH = D // HEADS
KC = D // P
HC = P // DH
TILES = GRAPHS * NODES // P
GT = 4
GROUPS = TILES // GT
SCALE = float(DH) ** -0.5
EPS = 1e-5
MASKED = -3.0e38
DMA = 16
LOOP = 2 * GT


def wait_for(eng, sem, count):
    if not isinstance(count, int) or count > 0:
        eng.wait_ge(sem, count)


def attention_kernel(nc, xt_dram, x_dram, adj_dram, w_dram, b_dram, out_dram):
    ctx = ExitStack()
    with ctx:
        def sb(name, shape, dt=F32):
            return ctx.enter_context(nc.sbuf_tensor(name, shape, dt))

        def sem(name):
            return ctx.enter_context(nc.semaphore(name))

        w_hi = [sb(f"w{n}_hi", [P, KC, D], F32R) for n in "qkvo"]
        w_lo = [sb(f"w{n}_lo", [P, KC, D], F32R) for n in "qkvo"]
        x_raw = sb("x_raw", [P, 2, KC, D])
        x_hi = sb("x_hi", [P, 2, KC, D], F32R)
        x_lo = sb("x_lo", [P, 2, KC, D], F32R)
        qt = sb("qt", [P, 2, KC, D])
        kt = sb("kt", [P, 2, KC, D])
        v = sb("v", [P, 2, GT, D])
        row = sb("row", [P, 4, D])
        soft = sb("soft", [P, 2, HEADS * NODES])
        pt = sb("pt", [P, HEADS, NODES])
        ot_hi = sb("ot_hi", [P, KC, P], F32R)
        ot_lo = sb("ot_lo", [P, KC, P], F32R)
        adj = sb("adj", [P, 2, GT, NODES], I32)
        bias = sb("bias", [P, 2, GT, NODES])
        bq = sb("bq", [P, KC])
        bk = sb("bk", [P, KC])
        bv = sb("bv", [P, D])
        bo = sb("bo", [P, D])
        ident = sb("ident", [P, P])
        top = sb("top", [P, 2, HEADS])
        total = sb("total", [P, 2, HEADS])
        inverse = sb("inverse", [P, 2, HEADS])
        stats = sb("stats", [P, 2, 6])
        moments = sb("moments", [P, 2, 2])
        shifted = sb("shifted", [P, 2, 1])
        rstd = sb("rstd", [P, 2, 1])
        eps = sb("eps", [P, 1])
        minus_half = sb("minus_half", [P, 1])

        attn = ctx.enter_context(nc.psum_tensor("attn", [P, 4, D], F32))
        psum_v = ctx.enter_context(nc.psum_tensor("psum_v", [P, D], F32))
        psum_q = ctx.enter_context(nc.psum_tensor("psum_q", [P, D], F32))
        psum_k = ctx.enter_context(nc.psum_tensor("psum_k", [P, D], F32))
        psum_y = ctx.enter_context(nc.psum_tensor("psum_y", [P, D], F32))

        w_in = [sem(f"w{n}_in") for n in "qkvo"]
        b_in = sem("b_in")
        x_in = [sem("x_in0"), sem("x_in1")]
        adj_in = [sem("adj_in0"), sem("adj_in1")]
        row_in = [sem(f"row_in{n}") for n in range(4)]
        stored = [sem(f"stored{n}") for n in range(4)]
        w_hi_done = sem("w_hi_done")
        w_lo_done = sem("w_lo_done")
        const_done = sem("const_done")
        ident_set = sem("ident_set")
        x_hi_done = sem("x_hi_done")
        x_lo_done = sem("x_lo_done")
        v_proj, q_proj, k_proj = sem("v_proj"), sem("q_proj"), sem("k_proj")
        v_done, q_done, k_done = sem("v_done"), sem("q_done"), sem("k_done")
        bias_done = sem("bias_done")
        scored = sem("scored")
        masked = sem("masked")
        topped = sem("topped")
        centred = sem("centred")
        exped = sem("exped")
        summed = sem("summed")
        inverted = sem("inverted")
        normed = sem("normed")
        transposed = sem("transposed")
        pt_done = sem("pt_done")
        mixed = sem("mixed")
        ot_hi_done = sem("ot_hi_done")
        ot_lo_done = sem("ot_lo_done")
        y_proj = sem("y_proj")
        row_biased = sem("row_biased")
        row_added = sem("row_added")
        row_stats = sem("row_stats")
        row_moments = sem("row_moments")
        row_shifted = sem("row_shifted")
        row_rstd = sem("row_rstd")
        row_done = sem("row_done")
        pe_went_on, dve_went_on, pool_went_on = sem("pe_went_on"), sem("dve_went_on"), sem("pool_went_on")

        w_raw = [qt[:, 1], kt[:, 1], v[:, 1], soft[:, :, :].rearrange("p a (c n) -> p (a c) n", n=D)]

        def by_head(ap):
            return ap.rearrange("p (h k) -> p h k", k=NODES)

        def run_slots(eng, slot, peeled):
            for c in range(GT):
                slot(0, c)
            with eng.Fori(0, (GROUPS - 1 - peeled) // 2) as i:
                for c in range(GT, GT + LOOP):
                    slot(i, c)
            for c in range(TILES - peeled * GT, TILES + 3):
                slot(0, c)

        block = ctx.enter_context(nc.Block())

        @block.sync
        def _(sp):
            def load_x(i, c):
                g, buf = 2 * i + c // GT, c // GT % 2
                sp.dma_start(x_raw[:, buf], xt_dram[g]).then_inc(x_in[buf], DMA)

            def load_adj(i, c):
                g, buf = 2 * i + c // GT, c // GT % 2
                sp.dma_start(adj[:, buf], adj_dram[g]).then_inc(adj_in[buf], DMA)

            sp.dma_start(w_raw[0], w_dram[0]).then_inc(w_in[0], DMA)
            load_x(0, 0)
            sp.dma_start(w_raw[1], w_dram[1]).then_inc(w_in[1], DMA)
            for dst, src in zip((bq, bk, bv, bo), b_dram):
                sp.dma_start(dst[:, :], src).then_inc(b_in, DMA)
            sp.dma_start(w_raw[2], w_dram[2]).then_inc(w_in[2], DMA)
            load_adj(0, 0)
            load_x(0, GT)
            sp.dma_start(w_raw[3], w_dram[3]).then_inc(w_in[3], DMA)
            sp.wait_ge(x_hi_done, KC)
            sp.wait_ge(x_lo_done, KC)
            load_x(0, 2 * GT)

            def slot(i, c):
                T = 8 * i + c
                if c % GT == 0 and c < TILES - GT:
                    wait_for(sp, bias_done, 2 * i + c // GT)
                    load_adj(i, c + GT)
                if c % GT == 0 and c < TILES - 3 * GT:
                    sp.wait_ge(x_hi_done, T + 2 * GT)
                    sp.wait_ge(x_lo_done, T + 2 * GT)
                    load_x(i, c + 3 * GT)
                if c >= 3:
                    sp.wait_ge(row_done, T - 2)
                    sp.dma_start(out_dram[T - 3], row[:, (c - 3) % 4]).then_inc(stored[(c - 3) % 4], DMA)
                if c < TILES:
                    if c >= 4:
                        sp.wait_ge(stored[c % 4], DMA * (2 * i + c // 4))
                    sp.dma_start(row[:, c % 4], x_dram[T]).then_inc(row_in[c % 4], DMA)

            run_slots(sp, slot, 3)
            for n in range(4):
                sp.wait_ge(stored[n], DMA * TILES // 4)

        @block.tensor
        def _(pe):
            def split_matmul(out, left_hi, left_lo, right_hi, right_lo):
                for kc in range(KC):
                    nc.tensor.matmul(out, left_hi(kc), right_hi(kc), start=kc == 0, stop=False)
                    nc.tensor.matmul(out, left_hi(kc), right_lo(kc), start=False, stop=False)
                    last = nc.tensor.matmul(out, left_lo(kc), right_hi(kc), start=False, stop=kc == KC - 1)
                return last

            def project_v(i, c):
                J, buf, t = 8 * i + c, c // GT % 2, c % GT
                if c % GT == 0:
                    pe.wait_ge(x_hi_done, J + GT)
                    pe.wait_ge(x_lo_done, J + GT)
                wait_for(pe, v_done, J)
                split_matmul(psum_v[:, :],
                             lambda kc: x_hi[:, buf, kc, t * P:(t + 1) * P],
                             lambda kc: x_lo[:, buf, kc, t * P:(t + 1) * P],
                             lambda kc: w_hi[2][:, kc, :],
                             lambda kc: w_lo[2][:, kc, :]).then_inc(v_proj, 1)

            def project_qk(i, c):
                J, buf, m = 8 * i + c, c // GT % 2, c % GT
                wait_for(pe, q_done, J)
                split_matmul(psum_q[:, :],
                             lambda kc: w_hi[0][:, kc, m * P:(m + 1) * P],
                             lambda kc: w_lo[0][:, kc, m * P:(m + 1) * P],
                             lambda kc: x_hi[:, buf, kc, :],
                             lambda kc: x_lo[:, buf, kc, :]).then_inc(q_proj, 1)
                wait_for(pe, k_done, J)
                split_matmul(psum_k[:, :],
                             lambda kc: w_hi[1][:, kc, m * P:(m + 1) * P],
                             lambda kc: w_lo[1][:, kc, m * P:(m + 1) * P],
                             lambda kc: x_hi[:, buf, kc, :],
                             lambda kc: x_lo[:, buf, kc, :]).then_inc(k_proj, 1)

            def score(i, c):
                T, buf, t = 8 * i + c, c // GT % 2, c % GT
                if t == 0:
                    pe.wait_ge(q_done, T + GT)
                    pe.wait_ge(k_done, T + GT)
                wait_for(pe, masked, T)
                wait_for(pe, pt_done, T - 1)
                wait_for(pe, ot_hi_done, T - 1)
                wait_for(pe, ot_lo_done, T - 1)
                for kc in range(KC):
                    for graph in range(2):
                        at = t * P + graph * NODES
                        for r in range(HC):
                            f = slice(r * DH, (r + 1) * DH)
                            last = nc.tensor.matmul(
                                attn[graph * NODES:(graph + 1) * NODES, r, kc * NODES:(kc + 1) * NODES],
                                qt[f, buf, kc, at:at + NODES], kt[f, buf, kc, at:at + NODES],
                                start=True, stop=True)
                last.then_inc(scored, 1)

            def transpose(i, c):
                T = 8 * i + c
                pe.wait_ge(normed, T + 1)
                for j in range(HEADS // 2):
                    last = nc.tensor.transpose(attn[:, j // 4, (j % 4) * P:(j % 4 + 1) * P],
                                               soft[:, c % 2, j * P:(j + 1) * P], ident[:, :])
                last.then_inc(transposed, 1)

            def mix(i, c):
                T, buf, t = 8 * i + c, c // GT % 2, c % GT
                pe.wait_ge(pt_done, T + 1)
                pe.wait_ge(v_done, T + 1)
                pe.sem_inc(pe_went_on, 1)
                for kc in range(KC):
                    for r in range(HC):
                        h = kc * HC + r
                        for graph in range(2):
                            keys = slice(graph * NODES, (graph + 1) * NODES)
                            last = nc.tensor.matmul(
                                attn[r * DH:(r + 1) * DH, 2 + graph, kc * NODES:(kc + 1) * NODES],
                                v[keys, buf, t, h * DH:(h + 1) * DH], pt[keys, r * KC + kc, :],
                                start=True, stop=True)
                last.then_inc(mixed, 1)

            def project_out(i, c):
                T = 8 * i + c
                pe.wait_ge(ot_hi_done, T + 1)
                pe.wait_ge(ot_lo_done, T + 1)
                wait_for(pe, row_added, T)
                split_matmul(psum_y[:, :],
                             lambda kc: ot_hi[:, kc, :], lambda kc: ot_lo[:, kc, :],
                             lambda kc: w_hi[3][:, kc, :], lambda kc: w_lo[3][:, kc, :]).then_inc(y_proj, 1)

            def slot(i, c):
                if c < TILES:
                    score(i, c)
                if c < TILES - GT:
                    project_v(i, c + GT)
                if c < TILES:
                    pe.wait_ge(masked, 8 * i + c + 1)
                if 1 <= c < TILES + 1:
                    transpose(i, c - 1)
                if 2 <= c < TILES + 2:
                    project_out(i, c - 2)
                if 1 <= c < TILES + 1:
                    mix(i, c - 1)
                if c < TILES - GT:
                    project_qk(i, c + GT)

            pe.wait_ge(w_hi_done, 2)
            pe.wait_ge(w_lo_done, 2)
            pe.wait_ge(x_hi_done, KC)
            pe.wait_ge(x_lo_done, KC)
            for c in range(GT):
                project_qk(0, c)
            pe.wait_ge(w_hi_done, 3)
            pe.wait_ge(w_lo_done, 3)
            for c in range(GT):
                project_v(0, c)
            pe.wait_ge(w_hi_done, 4)
            pe.wait_ge(w_lo_done, 4)
            pe.wait_ge(const_done, 1)
            run_slots(pe, slot, 1)

        @block.scalar
        def _(act):
            def split_x(i, c):
                buf, kc = c // GT % 2, c % GT
                if kc == 0:
                    act.wait_ge(x_in[buf], DMA * (i + c // GT // 2 + 1))
                if c >= 2 * GT and kc == 0:
                    act.wait_ge(k_proj, 8 * i + c - GT)
                    act.wait_ge(v_proj, 8 * i + c - GT)
                nc.scalar.copy(x_hi[:, buf, kc, :], x_raw[:, buf, kc, :]).then_inc(x_hi_done, 1)

            def read_qk(i, c):
                J, buf, m = 8 * i + c, c // GT % 2, c % GT
                act.wait_ge(q_proj, J + 1)
                if c >= 2 * GT:
                    act.wait_ge(scored, J - 2 * GT + 1 + (GT - 1 - m))
                nc.scalar.activation(qt[:, buf, m, :], psum_q[:, :], ACT.Identity,
                                     bias=bq[:, m:m + 1], scale=1.0).then_inc(q_done, 1)
                act.wait_ge(k_proj, J + 1)
                nc.scalar.activation(kt[:, buf, m, :], psum_k[:, :], ACT.Identity,
                                     bias=bk[:, m:m + 1], scale=1.0).then_inc(k_done, 1)

            def exp(i, c):
                T = 8 * i + c
                act.wait_ge(centred, T + 1)
                nc.scalar.activation(soft[:, c % 2, :], soft[:, c % 2, :], ACT.Exp,
                                     scale=SCALE).then_inc(exped, 1)

            def read_pt(i, c):
                T = 8 * i + c
                act.wait_ge(transposed, T + 1)
                wait_for(act, mixed, T)
                for half in range(2):
                    for graph in range(2):
                        src = attn[half * NODES:(half + 1) * NODES, 0:2, :].rearrange(
                            "p b (j q) -> p (b j) q", q=P)[:, :, graph * NODES:(graph + 1) * NODES]
                        dst = pt[graph * NODES:(graph + 1) * NODES, :, :].rearrange(
                            "p (j e) q -> p j e q", e=2)[:, :, half, :]
                        last = nc.scalar.copy(dst, src)
                last.then_inc(pt_done, 1)

            def read_ot(i, c):
                T = 8 * i + c
                act.wait_ge(mixed, T + 1)
                wait_for(act, y_proj, T)
                nc.scalar.copy(ot_hi[:, :, :].rearrange("p c (b q) -> p b c q", b=2),
                               attn[:, 2:4, 0:KC * NODES].rearrange("p b (c q) -> p b c q", q=NODES)
                               ).then_inc(ot_hi_done, 1)

            def slot(i, c):
                if c < TILES - 2 * GT:
                    split_x(i, c + 2 * GT)
                if 1 <= c < TILES + 1:
                    read_pt(i, c - 1)
                if c < TILES:
                    exp(i, c)
                if 1 <= c < TILES + 1:
                    read_ot(i, c - 1)
                if c < TILES - GT:
                    read_qk(i, c + GT)

            def split_w(n):
                act.wait_ge(w_in[n], DMA)
                nc.scalar.copy(w_hi[n][:, :, :], w_raw[n]).then_inc(w_hi_done, 1)

            split_w(0)
            for c in range(GT):
                split_x(0, c)
            split_w(1)
            act.wait_ge(b_in, DMA * 4)
            split_w(2)
            for c in range(GT):
                read_qk(0, c)
            for c in range(GT, 2 * GT):
                split_x(0, c)
            split_w(3)
            run_slots(act, slot, 3)

        @block.vector
        def _(dve):
            def split_x(i, c):
                buf, kc = c // GT % 2, c % GT
                dve.wait_ge(x_hi_done, 8 * i + c + 1)
                nc.vector.tensor_tensor(x_lo[:, buf, kc, :], x_raw[:, buf, kc, :],
                                        x_hi[:, buf, kc, :].bitcast(F32), ALU.subtract).then_inc(x_lo_done, 1)

            def read_v(i, c):
                J, buf, t = 8 * i + c, c // GT % 2, c % GT
                dve.wait_ge(v_proj, J + 1)
                wait_for(dve, mixed, J - 2 * GT + 1)
                nc.vector.tensor_tensor(v[:, buf, t, :], psum_v[:, :], bv[:, :], ALU.add).then_inc(v_done, 1)

            def mask(i, c):
                T = 8 * i + c
                if c % GT == 0:
                    dve.wait_ge(bias_done, 2 * i + c // GT + 1)
                dve.wait_ge(scored, T + 1)
                wait_for(dve, transposed, T - 1)
                nc.vector.tensor_tensor(
                    soft[:, c % 2, :].rearrange("p (r c k) -> p r c k", r=HC, k=NODES),
                    attn[:, :, 0:KC * NODES].rearrange("p r (c k) -> p r c k", k=NODES),
                    bias[:, c // GT % 2, c % GT, :].unsqueeze(1).unsqueeze(1).to_broadcast([P, HC, KC, NODES]),
                    ALU.add).then_inc(masked, 1)
                dve.wait_ge(masked, T + 1)
                nc.vector.tensor_reduce(top[:, c % 2, :], by_head(soft[:, c % 2, :]), AX_X,
                                        ALU.max).then_inc(topped, 1)

            def sum_up(i, c):
                T = 8 * i + c
                dve.wait_ge(exped, T + 1)
                nc.vector.tensor_reduce(total[:, c % 2, :], by_head(soft[:, c % 2, :]), AX_X,
                                        ALU.add).then_inc(summed, 1)
                dve.wait_ge(summed, T + 1)
                nc.vector.reciprocal(inverse[:, c % 2, :], total[:, c % 2, :]).then_inc(inverted, 1)

            def split_ot(i, c):
                T = 8 * i + c
                dve.wait_ge(ot_hi_done, T + 1)
                wait_for(dve, y_proj, T)
                nc.vector.tensor_tensor(
                    ot_lo[:, :, :].rearrange("p c (b q) -> p b c q", b=2),
                    attn[:, 2:4, 0:KC * NODES].rearrange("p b (c q) -> p b c q", q=NODES),
                    ot_hi[:, :, :].rearrange("p c (b q) -> p b c q", b=2).bitcast(F32),
                    ALU.subtract).then_inc(ot_lo_done, 1)

            def add_row(i, c):
                T = 8 * i + c
                dve.wait_ge(y_proj, T + 1)
                dve.wait_ge(row_biased, T + 1)
                nc.vector.tensor_tensor(row[:, c % 4, :], psum_y[:, :], row[:, c % 4, :],
                                        ALU.add).then_inc(row_added, 1)
                dve.wait_ge(row_added, T + 1)
                nc.vector.bn_stats(stats[:, c % 2, :], row[:, c % 4, :]).then_inc(row_stats, 1)
                dve.wait_ge(row_stats, T + 1)
                dve.sem_inc(dve_went_on, 1)
                nc.vector.bn_aggr(moments[:, c % 2, :], stats[:, c % 2, :]).then_inc(row_moments, 1)

            def norm_row(i, c):
                T = 8 * i + c
                dve.wait_ge(row_rstd, T + 1)
                nc.vector.tensor_scalar(row[:, c % 4, :], row[:, c % 4, :], moments[:, c % 2, 0:1],
                                        rstd[:, c % 2, :], ALU.subtract, ALU.mult).then_inc(row_done, 1)

            def slot(i, c):
                if c < TILES:
                    mask(i, c)
                if c < TILES - 2 * GT:
                    split_x(i, c + 2 * GT)
                if c < TILES - GT:
                    read_v(i, c + GT)
                if c >= 3:
                    norm_row(i, c - 3)
                if 2 <= c < TILES + 2:
                    add_row(i, c - 2)
                if c < TILES:
                    sum_up(i, c)
                if 1 <= c < TILES + 1:
                    split_ot(i, c - 1)

            def split_w(n):
                dve.wait_ge(w_hi_done, n + 1)
                nc.vector.tensor_tensor(w_lo[n][:, :, :], w_raw[n], w_hi[n][:, :, :].bitcast(F32),
                                        ALU.subtract).then_inc(w_lo_done, 1)

            split_w(0)
            for c in range(GT):
                split_x(0, c)
            split_w(1)
            split_w(2)
            dve.wait_ge(b_in, DMA * 4)
            for c in range(GT):
                read_v(0, c)
            for c in range(GT, 2 * GT):
                split_x(0, c)
            split_w(3)
            dve.wait_ge(w_lo_done, 4)
            run_slots(dve, slot, 3)

        @block.gpsimd
        def _(pool):
            def make_bias(i, c):
                g, buf = 2 * i + c // GT, c // GT % 2
                pool.wait_ge(adj_in[buf], DMA * (i + c // GT // 2 + 1))
                if c >= 2 * GT:
                    pool.wait_ge(masked, 4 * g - GT)
                pool.sem_inc(pool_went_on, 1)
                nc.gpsimd.tensor_scalar(bias[:, buf], adj[:, buf], 0.0, MASKED, ALU.is_equal,
                                        ALU.mult).then_inc(bias_done, 1)

            def add_bo(i, c):
                T = 8 * i + c
                pool.wait_ge(row_in[c % 4], DMA * (2 * i + c // 4 + 1))
                nc.gpsimd.tensor_tensor(row[:, c % 4, :], row[:, c % 4, :], bo[:, :],
                                        ALU.add).then_inc(row_biased, 1)

            def centre(i, c):
                T = 8 * i + c
                pool.wait_ge(topped, T + 1)
                nc.gpsimd.tensor_tensor(by_head(soft[:, c % 2, :]), by_head(soft[:, c % 2, :]),
                                        top[:, c % 2, :].unsqueeze(2).to_broadcast([P, HEADS, NODES]),
                                        ALU.subtract).then_inc(centred, 1)

            def norm(i, c):
                T = 8 * i + c
                pool.wait_ge(inverted, T + 1)
                nc.gpsimd.tensor_tensor(by_head(soft[:, c % 2, :]), by_head(soft[:, c % 2, :]),
                                        inverse[:, c % 2, :].unsqueeze(2).to_broadcast([P, HEADS, NODES]),
                                        ALU.mult).then_inc(normed, 1)

            def make_rstd(i, c):
                T = 8 * i + c
                pool.wait_ge(row_moments, T + 1)
                nc.gpsimd.tensor_tensor(shifted[:, c % 2, :], moments[:, c % 2, 1:2], eps[:, :],
                                        ALU.add).then_inc(row_shifted, 1)
                pool.wait_ge(row_shifted, T + 1)
                nc.gpsimd.tensor_tensor(rstd[:, c % 2, :], shifted[:, c % 2, :], minus_half[:, :],
                                        ALU.pow).then_inc(row_rstd, 1)

            def slot(i, c):
                if c % GT == 1 and c < TILES - GT:
                    make_bias(i, c + GT)
                if c < TILES:
                    add_bo(i, c)
                    centre(i, c)
                if 2 <= c < TILES + 2:
                    make_rstd(i, c - 2)
                if c < TILES:
                    norm(i, c)

            nc.gpsimd.memset(eps[:, :], EPS)
            nc.gpsimd.memset(minus_half[:, :], -0.5)
            nc.gpsimd.memset(ident[:, :], 0.0).then_inc(ident_set, 1)
            pool.wait_ge(ident_set, 1)
            nc.gpsimd.affine_select(out=ident[:, :], in_=ident[:, :], compare_op=ALU.not_equal, fill=1.0,
                                    base=0, pattern=[[-1, P]], channel_multiplier=1).then_inc(const_done, 1)
            pool.wait_ge(const_done, 1)
            make_bias(0, 0)
            pool.wait_ge(b_in, DMA * 4)
            run_slots(pool, slot, 1)


_SHAPES = {"xt": (GROUPS, P, KC, D), "x": (TILES, P, D), "adj": (GROUPS, P, GT, NODES)}


def kernel(x, adj, L0_gnn_Wq, L0_gnn_bq, L0_gnn_Wk, L0_gnn_bk, L0_gnn_Wv, L0_gnn_bv, L0_gnn_Wo, L0_gnn_bo):
    import numpy as np
    import concourse.bacc as bacc
    from concourse.bass_utils import run_bass_kernel_spmd

    x, adj = np.asarray(x), np.asarray(adj)
    rows = x.reshape(TILES, P, D)
    arrays = {
        "xt": np.ascontiguousarray(x.reshape(GROUPS, GT * P, KC, P).transpose(0, 3, 2, 1)),
        "x": np.ascontiguousarray(rows),
        "adj": np.ascontiguousarray(adj.reshape(GROUPS, GT, P, NODES).transpose(0, 2, 1, 3)),
    }
    for name, w in zip("qkvo", (L0_gnn_Wq, L0_gnn_Wk, L0_gnn_Wv, L0_gnn_Wo)):
        arrays["w" + name] = np.ascontiguousarray(np.asarray(w).reshape(KC, P, D).transpose(1, 0, 2))
    for name, b in zip("qkvo", (L0_gnn_bq, L0_gnn_bk, L0_gnn_bv, L0_gnn_bo)):
        b = np.asarray(b)
        arrays["b" + name] = np.ascontiguousarray(b.reshape(KC, P).T if name in "qk" else b.reshape(1, D))
    arrays = {f"in_{n}": a for n, a in arrays.items()}

    nc = bacc.Bacc("TRN2", target_bir_lowering=False, num_devices=1)
    dram = {n: nc.dram_tensor(n, a.shape, mybir.dt.from_np(a.dtype), kind="ExternalInput").ap()
            for n, a in arrays.items()}
    out = nc.dram_tensor("out_rows", (TILES, P, D), F32, kind="ExternalOutput").ap()
    by_feature = [dram[f"in_b{n}"] for n in "qk"]
    on_all_rows = [dram[f"in_b{n}"].to_broadcast([P, D]) for n in "vo"]
    attention_kernel(nc, dram["in_xt"], dram["in_x"], dram["in_adj"], [dram[f"in_w{n}"] for n in "qkvo"],
                     by_feature + on_all_rows, out)
    result = run_bass_kernel_spmd(nc, [arrays], core_ids=[0])
    return result.results[0]["out_rows"].reshape(GRAPHS, NODES, D)
```

```python
from contextlib import ExitStack

import concourse.bass as bass
from concourse import mybir

F32 = mybir.dt.float32
F32R = mybir.dt.float32r
I32 = mybir.dt.int32
ALU = mybir.AluOpType
ACT = mybir.ActivationFunctionType
AX_X = mybir.AxisListType.X

P = 128
GRAPHS, NODES, D = 128, 64, 512
HEADS = 16
DH = D // HEADS
KC = D // P
HC = P // DH
TILES = GRAPHS * NODES // P
GT = 4
GROUPS = TILES // GT
SCALE = float(DH) ** -0.5
EPS = 1e-5
MASKED = -3.0e38
DMA = 16
LOOP = 2 * GT
START = [("q", 0), ("q", 1), ("k", 0), ("q", 2), ("k", 1), ("q", 3), ("k", 2), ("k", 3)]


def wait_for(eng, sem, count):
    if not isinstance(count, int) or count > 0:
        eng.wait_ge(sem, count)


def attention_kernel(nc, xt_dram, x_dram, adj_dram, w_dram, b_dram, out_dram):
    ctx = ExitStack()
    with ctx:
        def sb(name, shape, dt=F32):
            return ctx.enter_context(nc.sbuf_tensor(name, shape, dt))

        def sem(name):
            return ctx.enter_context(nc.semaphore(name))

        w_hi = [sb(f"w{n}_hi", [P, KC, D], F32R) for n in "qkvo"]
        w_lo = [sb(f"w{n}_lo", [P, KC, D], F32R) for n in "qkvo"]
        x_raw = sb("x_raw", [P, 2, KC, D])
        x_hi = sb("x_hi", [P, 2, KC, D], F32R)
        x_lo = sb("x_lo", [P, 2, KC, D], F32R)
        qt = sb("qt", [P, 2, KC, D])
        kt = sb("kt", [P, 2, KC, D])
        v = sb("v", [P, 2, GT, D])
        row = sb("row", [P, 4, D])
        soft = sb("soft", [P, 2, HEADS * NODES])
        pt = sb("pt", [P, HEADS, NODES])
        ot_hi = sb("ot_hi", [P, KC, P], F32R)
        ot_lo = sb("ot_lo", [P, KC, P], F32R)
        adj = sb("adj", [P, 2, GT, NODES], I32)
        bias = sb("bias", [P, 2, GT, NODES])
        bq = sb("bq", [P, KC])
        bk = sb("bk", [P, KC])
        bv = sb("bv", [P, D])
        bo = sb("bo", [P, D])
        ident = sb("ident", [P, P])
        top = sb("top", [P, 2, HEADS])
        total = sb("total", [P, 2, HEADS])
        inverse = sb("inverse", [P, 2, HEADS])
        stats = sb("stats", [P, 2, 6])
        moments = sb("moments", [P, 2, 2])
        shifted = sb("shifted", [P, 2, 1])
        rstd = sb("rstd", [P, 2, 1])
        eps = sb("eps", [P, 1])
        minus_half = sb("minus_half", [P, 1])

        attn = ctx.enter_context(nc.psum_tensor("attn", [P, 4, D], F32))
        psum_v = ctx.enter_context(nc.psum_tensor("psum_v", [P, D], F32))
        psum_q = ctx.enter_context(nc.psum_tensor("psum_q", [P, D], F32))
        psum_k = ctx.enter_context(nc.psum_tensor("psum_k", [P, D], F32))
        psum_y = ctx.enter_context(nc.psum_tensor("psum_y", [P, D], F32))

        wq_in = [sem(f"wq_in{n}") for n in range(KC)]
        x0_in = [sem(f"x0_in{n}") for n in range(KC)]
        w_in = [None] + [sem(f"w{n}_in") for n in "kvo"]
        b_in = sem("b_in")
        x_in = [sem("x_in0"), sem("x_in1")]
        adj_in = [sem("adj_in0"), sem("adj_in1")]
        row_in = [sem(f"row_in{n}") for n in range(4)]
        stored = [sem(f"stored{n}") for n in range(4)]
        w_hi_done = sem("w_hi_done")
        w_lo_done = sem("w_lo_done")
        const_done = sem("const_done")
        ident_set = sem("ident_set")
        x_hi_done = sem("x_hi_done")
        x_lo_done = sem("x_lo_done")
        v_proj, q_proj, k_proj = sem("v_proj"), sem("q_proj"), sem("k_proj")
        v_done, q_done, k_done = sem("v_done"), sem("q_done"), sem("k_done")
        bias_done = sem("bias_done")
        scored = sem("scored")
        masked = sem("masked")
        topped = sem("topped")
        centred = sem("centred")
        exped = sem("exped")
        summed = sem("summed")
        inverted = sem("inverted")
        normed = sem("normed")
        transposed = sem("transposed")
        pt_done = sem("pt_done")
        mixed = sem("mixed")
        ot_hi_done = sem("ot_hi_done")
        ot_lo_done = sem("ot_lo_done")
        y_proj = sem("y_proj")
        row_biased = sem("row_biased")
        row_added = sem("row_added")
        row_stats = sem("row_stats")
        row_moments = sem("row_moments")
        row_shifted = sem("row_shifted")
        row_rstd = sem("row_rstd")
        row_done = sem("row_done")
        pe_went_on, dve_went_on, pool_went_on = sem("pe_went_on"), sem("dve_went_on"), sem("pool_went_on")

        w_raw = [qt[:, 1], kt[:, 1], v[:, 1], soft[:, :, :].rearrange("p a (c n) -> p (a c) n", n=D)]

        def by_head(ap):
            return ap.rearrange("p (h k) -> p h k", k=NODES)

        def run_slots(eng, slot, peeled):
            for c in range(GT):
                slot(0, c)
            with eng.Fori(0, (GROUPS - 1 - peeled) // 2) as i:
                for c in range(GT, GT + LOOP):
                    slot(i, c)
            for c in range(TILES - peeled * GT, TILES + 3):
                slot(0, c)

        block = ctx.enter_context(nc.Block())

        @block.sync
        def _(sp):
            def load_x(i, c):
                g, buf = 2 * i + c // GT, c // GT % 2
                sp.dma_start(x_raw[:, buf], xt_dram[g]).then_inc(x_in[buf], DMA)

            def load_adj(i, c):
                g, buf = 2 * i + c // GT, c // GT % 2
                sp.dma_start(adj[:, buf], adj_dram[g]).then_inc(adj_in[buf], DMA)

            for kc in range(KC):
                sp.dma_start(w_raw[0][:, kc, :], w_dram[0][:, kc, :]).then_inc(wq_in[kc], DMA)
                sp.dma_start(x_raw[:, 0, kc, :], xt_dram[0, :, kc, :]).then_inc(x0_in[kc], DMA)
            sp.dma_start(w_raw[1], w_dram[1]).then_inc(w_in[1], DMA)
            for dst, src in zip((bq, bk, bv, bo), b_dram):
                sp.dma_start(dst[:, :], src).then_inc(b_in, DMA)
            sp.dma_start(w_raw[2], w_dram[2]).then_inc(w_in[2], DMA)
            load_adj(0, 0)
            load_x(0, GT)
            sp.dma_start(w_raw[3], w_dram[3]).then_inc(w_in[3], DMA)
            sp.wait_ge(x_hi_done, KC)
            sp.wait_ge(x_lo_done, KC)
            load_x(0, 2 * GT)

            def slot(i, c):
                T = 8 * i + c
                if c % GT == 0 and c < TILES - GT:
                    wait_for(sp, bias_done, 2 * i + c // GT)
                    load_adj(i, c + GT)
                if c % GT == 0 and c < TILES - 3 * GT:
                    sp.wait_ge(x_hi_done, T + 2 * GT)
                    sp.wait_ge(x_lo_done, T + 2 * GT)
                    load_x(i, c + 3 * GT)
                if c >= 3:
                    sp.wait_ge(row_done, T - 2)
                    sp.dma_start(out_dram[T - 3], row[:, (c - 3) % 4]).then_inc(stored[(c - 3) % 4], DMA)
                if c < TILES:
                    if c >= 4:
                        sp.wait_ge(stored[c % 4], DMA * (2 * i + c // 4))
                    sp.dma_start(row[:, c % 4], x_dram[T]).then_inc(row_in[c % 4], DMA)

            run_slots(sp, slot, 3)
            for n in range(4):
                sp.wait_ge(stored[n], DMA * TILES // 4)

        @block.tensor
        def _(pe):
            def split_matmul(out, kc, left_hi, left_lo, right_hi, right_lo):
                nc.tensor.matmul(out, left_hi, right_hi, start=kc == 0, stop=False)
                nc.tensor.matmul(out, left_hi, right_lo, start=False, stop=False)
                return nc.tensor.matmul(out, left_lo, right_hi, start=False, stop=kc == KC - 1)

            def project_v(i, c, kc):
                J, buf, at = 8 * i + c, c // GT % 2, slice(c % GT * P, (c % GT + 1) * P)
                if kc == 0:
                    if c % GT == 0:
                        pe.wait_ge(x_hi_done, J + GT)
                        pe.wait_ge(x_lo_done, J + GT)
                    wait_for(pe, v_done, J)
                last = split_matmul(psum_v[:, :], kc, x_hi[:, buf, kc, at], x_lo[:, buf, kc, at],
                                    w_hi[2][:, kc, :], w_lo[2][:, kc, :])
                if kc == KC - 1:
                    last.then_inc(v_proj, 1)

            def project_q(i, c):
                J, buf, m = 8 * i + c, c // GT % 2, slice(c % GT * P, (c % GT + 1) * P)
                wait_for(pe, q_done, J)
                for kc in range(KC):
                    if isinstance(i, int) and c == 0:
                        pe.wait_ge(w_hi_done, kc + 1)
                        pe.wait_ge(w_lo_done, kc + 1)
                        pe.wait_ge(x_hi_done, kc + 1)
                        pe.wait_ge(x_lo_done, kc + 1)
                    last = split_matmul(psum_q[:, :], kc, w_hi[0][:, kc, m], w_lo[0][:, kc, m],
                                        x_hi[:, buf, kc, :], x_lo[:, buf, kc, :])
                last.then_inc(q_proj, 1)

            def project_k(i, c):
                J, buf, m = 8 * i + c, c // GT % 2, slice(c % GT * P, (c % GT + 1) * P)
                wait_for(pe, k_done, J)
                for kc in range(KC):
                    if isinstance(i, int) and c == 0:
                        pe.wait_ge(w_hi_done, KC + kc + 1)
                        pe.wait_ge(w_lo_done, KC + kc + 1)
                    last = split_matmul(psum_k[:, :], kc, w_hi[1][:, kc, m], w_lo[1][:, kc, m],
                                        x_hi[:, buf, kc, :], x_lo[:, buf, kc, :])
                last.then_inc(k_proj, 1)

            def score(i, c, kc):
                T, buf, t = 8 * i + c, c // GT % 2, c % GT
                if t == 0:
                    pe.wait_ge(q_done, T + kc + 1)
                    pe.wait_ge(k_done, T + kc + 1)
                if kc == 0:
                    wait_for(pe, masked, T)
                    wait_for(pe, pt_done, T - 1)
                    wait_for(pe, ot_hi_done, T - 1)
                    wait_for(pe, ot_lo_done, T - 1)
                for graph in range(2):
                    rows = slice(t * P + graph * NODES, t * P + (graph + 1) * NODES)
                    for r in range(HC):
                        f = slice(r * DH, (r + 1) * DH)
                        last = nc.tensor.matmul(
                            attn[graph * NODES:(graph + 1) * NODES, r, kc * NODES:(kc + 1) * NODES],
                            qt[f, buf, kc, rows], kt[f, buf, kc, rows], start=True, stop=True)
                if kc == KC - 1:
                    last.then_inc(scored, 1)

            def transpose(i, c):
                T = 8 * i + c
                pe.wait_ge(normed, T + 1)
                for j in range(HEADS // 2):
                    last = nc.tensor.transpose(attn[:, j // 4, (j % 4) * P:(j % 4 + 1) * P],
                                               soft[:, c % 2, j * P:(j + 1) * P], ident[:, :])
                last.then_inc(transposed, 1)

            def mix(i, c):
                T, buf, t = 8 * i + c, c // GT % 2, c % GT
                pe.wait_ge(pt_done, T + 1)
                pe.wait_ge(v_done, T + 1)
                pe.sem_inc(pe_went_on, 1)
                for kc in range(KC):
                    for r in range(HC):
                        h = kc * HC + r
                        for graph in range(2):
                            keys = slice(graph * NODES, (graph + 1) * NODES)
                            last = nc.tensor.matmul(
                                attn[r * DH:(r + 1) * DH, 2 + graph, kc * NODES:(kc + 1) * NODES],
                                v[keys, buf, t, h * DH:(h + 1) * DH], pt[keys, r * KC + kc, :],
                                start=True, stop=True)
                last.then_inc(mixed, 1)

            def project_out(i, c):
                T = 8 * i + c
                pe.wait_ge(ot_hi_done, T + 1)
                pe.wait_ge(ot_lo_done, T + 1)
                wait_for(pe, row_added, T)
                for kc in range(KC):
                    last = split_matmul(psum_y[:, :], kc, ot_hi[:, kc, :], ot_lo[:, kc, :],
                                        w_hi[3][:, kc, :], w_lo[3][:, kc, :])
                last.then_inc(y_proj, 1)

            def slot(i, c):
                for kc in range(KC):
                    if c < TILES:
                        score(i, c, kc)
                    if c < TILES - GT:
                        project_v(i, c + GT, kc)
                if 2 <= c < TILES + 2:
                    project_out(i, c - 2)
                if c < TILES:
                    pe.wait_ge(masked, 8 * i + c + 1)
                if 1 <= c < TILES + 1:
                    transpose(i, c - 1)
                if c < TILES - GT:
                    project_q(i, c + GT)
                if 1 <= c < TILES + 1:
                    mix(i, c - 1)
                if c < TILES - GT:
                    project_k(i, c + GT)

            for project, c in START:
                (project_q if project == "q" else project_k)(0, c)
            pe.wait_ge(w_hi_done, 3 * KC)
            pe.wait_ge(w_lo_done, 3 * KC)
            for c in range(GT):
                for kc in range(KC):
                    project_v(0, c, kc)
            pe.wait_ge(w_hi_done, 4 * KC)
            pe.wait_ge(w_lo_done, 4 * KC)
            pe.wait_ge(const_done, 1)
            run_slots(pe, slot, 1)

        @block.scalar
        def _(act):
            def split_x(i, c):
                buf, kc = c // GT % 2, c % GT
                if kc == 0:
                    act.wait_ge(x_in[buf], DMA * (i + c // GT // 2 + (1 if buf else 0)))
                if c >= 2 * GT and kc == 0:
                    act.wait_ge(k_proj, 8 * i + c - GT)
                    act.wait_ge(v_proj, 8 * i + c - GT)
                nc.scalar.copy(x_hi[:, buf, kc, :], x_raw[:, buf, kc, :]).then_inc(x_hi_done, 1)

            def read_q(i, c):
                J, buf, m = 8 * i + c, c // GT % 2, c % GT
                act.wait_ge(q_proj, J + 1)
                if c >= 2 * GT:
                    act.wait_ge(scored, J - m - GT)
                nc.scalar.activation(qt[:, buf, m, :], psum_q[:, :], ACT.Identity,
                                     bias=bq[:, m:m + 1], scale=1.0).then_inc(q_done, 1)

            def read_k(i, c):
                J, buf, m = 8 * i + c, c // GT % 2, c % GT
                act.wait_ge(k_proj, J + 1)
                if c >= 2 * GT:
                    act.wait_ge(scored, J - m - GT)
                nc.scalar.activation(kt[:, buf, m, :], psum_k[:, :], ACT.Identity,
                                     bias=bk[:, m:m + 1], scale=1.0).then_inc(k_done, 1)

            def exp(i, c):
                T = 8 * i + c
                act.wait_ge(centred, T + 1)
                nc.scalar.activation(soft[:, c % 2, :], soft[:, c % 2, :], ACT.Exp,
                                     scale=SCALE).then_inc(exped, 1)

            def read_pt(i, c):
                T = 8 * i + c
                act.wait_ge(transposed, T + 1)
                wait_for(act, mixed, T)
                for half in range(2):
                    for graph in range(2):
                        src = attn[half * NODES:(half + 1) * NODES, 0:2, :].rearrange(
                            "p b (j q) -> p (b j) q", q=P)[:, :, graph * NODES:(graph + 1) * NODES]
                        dst = pt[graph * NODES:(graph + 1) * NODES, :, :].rearrange(
                            "p (j e) q -> p j e q", e=2)[:, :, half, :]
                        last = nc.scalar.copy(dst, src)
                last.then_inc(pt_done, 1)

            def read_ot(i, c):
                T = 8 * i + c
                act.wait_ge(mixed, T + 1)
                wait_for(act, y_proj, T)
                nc.scalar.copy(ot_hi[:, :, :].rearrange("p c (b q) -> p b c q", b=2),
                               attn[:, 2:4, 0:KC * NODES].rearrange("p b (c q) -> p b c q", q=NODES)
                               ).then_inc(ot_hi_done, 1)

            def slot(i, c):
                if c < TILES - 2 * GT:
                    split_x(i, c + 2 * GT)
                if 1 <= c < TILES + 1:
                    read_pt(i, c - 1)
                if c < TILES:
                    exp(i, c)
                if c < TILES - GT:
                    read_q(i, c + GT)
                if 1 <= c < TILES + 1:
                    read_ot(i, c - 1)
                if c < TILES - GT:
                    read_k(i, c + GT)

            def split_w(n, kc):
                if n == 0:
                    act.wait_ge(wq_in[kc], DMA)
                elif kc == 0:
                    act.wait_ge(w_in[n], DMA)
                nc.scalar.copy(w_hi[n][:, kc, :], w_raw[n][:, kc, :]).then_inc(w_hi_done, 1)

            for kc in range(KC):
                split_w(0, kc)
                act.wait_ge(x0_in[kc], DMA)
                nc.scalar.copy(x_hi[:, 0, kc, :], x_raw[:, 0, kc, :]).then_inc(x_hi_done, 1)
            for kc in range(KC):
                split_w(1, kc)
            act.wait_ge(b_in, DMA * 4)
            for n, (project, c) in enumerate(START):
                (read_q if project == "q" else read_k)(0, c)
                if n < KC:
                    split_w(2, n)
            for c in range(GT, 2 * GT):
                split_x(0, c)
            for kc in range(KC):
                split_w(3, kc)
            run_slots(act, slot, 3)

        @block.vector
        def _(dve):
            def split_x(i, c):
                buf, kc = c // GT % 2, c % GT
                dve.wait_ge(x_hi_done, 8 * i + c + 1)
                nc.vector.tensor_tensor(x_lo[:, buf, kc, :], x_raw[:, buf, kc, :],
                                        x_hi[:, buf, kc, :].bitcast(F32), ALU.subtract).then_inc(x_lo_done, 1)

            def read_v(i, c):
                J, buf, t = 8 * i + c, c // GT % 2, c % GT
                dve.wait_ge(v_proj, J + 1)
                wait_for(dve, mixed, J - 2 * GT + 1)
                nc.vector.tensor_tensor(v[:, buf, t, :], psum_v[:, :], bv[:, :], ALU.add).then_inc(v_done, 1)

            def mask(i, c):
                T = 8 * i + c
                if c % GT == 0:
                    dve.wait_ge(bias_done, 2 * i + c // GT + 1)
                dve.wait_ge(scored, T + 1)
                wait_for(dve, transposed, T - 1)
                nc.vector.tensor_tensor(
                    soft[:, c % 2, :].rearrange("p (r c k) -> p r c k", r=HC, k=NODES),
                    attn[:, :, 0:KC * NODES].rearrange("p r (c k) -> p r c k", k=NODES),
                    bias[:, c // GT % 2, c % GT, :].unsqueeze(1).unsqueeze(1).to_broadcast([P, HC, KC, NODES]),
                    ALU.add).then_inc(masked, 1)
                dve.wait_ge(masked, T + 1)
                nc.vector.tensor_reduce(top[:, c % 2, :], by_head(soft[:, c % 2, :]), AX_X,
                                        ALU.max).then_inc(topped, 1)

            def sum_up(i, c):
                T = 8 * i + c
                dve.wait_ge(exped, T + 1)
                nc.vector.tensor_reduce(total[:, c % 2, :], by_head(soft[:, c % 2, :]), AX_X,
                                        ALU.add).then_inc(summed, 1)
                dve.wait_ge(summed, T + 1)
                nc.vector.reciprocal(inverse[:, c % 2, :], total[:, c % 2, :]).then_inc(inverted, 1)

            def split_ot(i, c):
                T = 8 * i + c
                dve.wait_ge(ot_hi_done, T + 1)
                wait_for(dve, y_proj, T)
                nc.vector.tensor_tensor(
                    ot_lo[:, :, :].rearrange("p c (b q) -> p b c q", b=2),
                    attn[:, 2:4, 0:KC * NODES].rearrange("p b (c q) -> p b c q", q=NODES),
                    ot_hi[:, :, :].rearrange("p c (b q) -> p b c q", b=2).bitcast(F32),
                    ALU.subtract).then_inc(ot_lo_done, 1)

            def add_row(i, c):
                T = 8 * i + c
                dve.wait_ge(y_proj, T + 1)
                dve.wait_ge(row_biased, T + 1)
                nc.vector.tensor_tensor(row[:, c % 4, :], psum_y[:, :], row[:, c % 4, :],
                                        ALU.add).then_inc(row_added, 1)
                dve.wait_ge(row_added, T + 1)
                nc.vector.bn_stats(stats[:, c % 2, :], row[:, c % 4, :]).then_inc(row_stats, 1)
                dve.wait_ge(row_stats, T + 1)
                dve.sem_inc(dve_went_on, 1)
                nc.vector.bn_aggr(moments[:, c % 2, :], stats[:, c % 2, :]).then_inc(row_moments, 1)

            def norm_row(i, c):
                T = 8 * i + c
                dve.wait_ge(row_rstd, T + 1)
                nc.vector.tensor_scalar(row[:, c % 4, :], row[:, c % 4, :], moments[:, c % 2, 0:1],
                                        rstd[:, c % 2, :], ALU.subtract, ALU.mult).then_inc(row_done, 1)

            def slot(i, c):
                if c >= 3:
                    norm_row(i, c - 3)
                if c < TILES - 2 * GT:
                    split_x(i, c + 2 * GT)
                if c < TILES:
                    mask(i, c)
                if c < TILES - GT:
                    read_v(i, c + GT)
                if 2 <= c < TILES + 2:
                    add_row(i, c - 2)
                if c < TILES:
                    sum_up(i, c)
                if 1 <= c < TILES + 1:
                    split_ot(i, c - 1)

            def split_w(n, kc):
                dve.wait_ge(w_hi_done, n * KC + kc + 1)
                nc.vector.tensor_tensor(w_lo[n][:, kc, :], w_raw[n][:, kc, :],
                                        w_hi[n][:, kc, :].bitcast(F32), ALU.subtract).then_inc(w_lo_done, 1)

            for c in range(GT):
                split_w(0, c)
                split_x(0, c)
            for n in (1, 2):
                for kc in range(KC):
                    split_w(n, kc)
            dve.wait_ge(b_in, DMA * 4)
            for c in range(GT):
                read_v(0, c)
            for c in range(GT, 2 * GT):
                split_x(0, c)
            for kc in range(KC):
                split_w(3, kc)
            dve.wait_ge(w_lo_done, 4 * KC)
            run_slots(dve, slot, 3)

        @block.gpsimd
        def _(pool):
            def make_bias(i, c):
                g, buf = 2 * i + c // GT, c // GT % 2
                pool.wait_ge(adj_in[buf], DMA * (i + c // GT // 2 + 1))
                if c >= 2 * GT:
                    pool.wait_ge(masked, 4 * g - GT)
                pool.sem_inc(pool_went_on, 1)
                nc.gpsimd.tensor_scalar(bias[:, buf], adj[:, buf], 0.0, MASKED, ALU.is_equal,
                                        ALU.mult).then_inc(bias_done, 1)

            def add_bo(i, c):
                T = 8 * i + c
                pool.wait_ge(row_in[c % 4], DMA * (2 * i + c // 4 + 1))
                nc.gpsimd.tensor_tensor(row[:, c % 4, :], row[:, c % 4, :], bo[:, :],
                                        ALU.add).then_inc(row_biased, 1)

            def centre(i, c):
                T = 8 * i + c
                pool.wait_ge(topped, T + 1)
                nc.gpsimd.tensor_tensor(by_head(soft[:, c % 2, :]), by_head(soft[:, c % 2, :]),
                                        top[:, c % 2, :].unsqueeze(2).to_broadcast([P, HEADS, NODES]),
                                        ALU.subtract).then_inc(centred, 1)

            def norm(i, c):
                T = 8 * i + c
                pool.wait_ge(inverted, T + 1)
                nc.gpsimd.tensor_tensor(by_head(soft[:, c % 2, :]), by_head(soft[:, c % 2, :]),
                                        inverse[:, c % 2, :].unsqueeze(2).to_broadcast([P, HEADS, NODES]),
                                        ALU.mult).then_inc(normed, 1)

            def make_rstd(i, c):
                T = 8 * i + c
                pool.wait_ge(row_moments, T + 1)
                nc.gpsimd.tensor_tensor(shifted[:, c % 2, :], moments[:, c % 2, 1:2], eps[:, :],
                                        ALU.add).then_inc(row_shifted, 1)
                pool.wait_ge(row_shifted, T + 1)
                nc.gpsimd.tensor_tensor(rstd[:, c % 2, :], shifted[:, c % 2, :], minus_half[:, :],
                                        ALU.pow).then_inc(row_rstd, 1)

            def slot(i, c):
                if c % GT == 1 and c < TILES - GT:
                    make_bias(i, c + GT)
                if c < TILES:
                    centre(i, c)
                if 2 <= c < TILES + 2:
                    make_rstd(i, c - 2)
                if c < TILES:
                    norm(i, c)
                    add_bo(i, c)

            nc.gpsimd.memset(eps[:, :], EPS)
            nc.gpsimd.memset(minus_half[:, :], -0.5)
            nc.gpsimd.memset(ident[:, :], 0.0).then_inc(ident_set, 1)
            pool.wait_ge(ident_set, 1)
            nc.gpsimd.affine_select(out=ident[:, :], in_=ident[:, :], compare_op=ALU.not_equal, fill=1.0,
                                    base=0, pattern=[[-1, P]], channel_multiplier=1).then_inc(const_done, 1)
            pool.wait_ge(const_done, 1)
            make_bias(0, 0)
            pool.wait_ge(b_in, DMA * 4)
            run_slots(pool, slot, 1)


_SHAPES = {"xt": (GROUPS, P, KC, D), "x": (TILES, P, D), "adj": (GROUPS, P, GT, NODES)}


def kernel(x, adj, L0_gnn_Wq, L0_gnn_bq, L0_gnn_Wk, L0_gnn_bk, L0_gnn_Wv, L0_gnn_bv, L0_gnn_Wo, L0_gnn_bo):
    import numpy as np
    import concourse.bacc as bacc
    from concourse.bass_utils import run_bass_kernel_spmd

    x, adj = np.asarray(x), np.asarray(adj)
    rows = x.reshape(TILES, P, D)
    arrays = {
        "xt": np.ascontiguousarray(x.reshape(GROUPS, GT * P, KC, P).transpose(0, 3, 2, 1)),
        "x": np.ascontiguousarray(rows),
        "adj": np.ascontiguousarray(adj.reshape(GROUPS, GT, P, NODES).transpose(0, 2, 1, 3)),
    }
    for name, w in zip("qkvo", (L0_gnn_Wq, L0_gnn_Wk, L0_gnn_Wv, L0_gnn_Wo)):
        arrays["w" + name] = np.ascontiguousarray(np.asarray(w).reshape(KC, P, D).transpose(1, 0, 2))
    for name, b in zip("qkvo", (L0_gnn_bq, L0_gnn_bk, L0_gnn_bv, L0_gnn_bo)):
        b = np.asarray(b)
        arrays["b" + name] = np.ascontiguousarray(b.reshape(KC, P).T if name in "qk" else b.reshape(1, D))
    arrays = {f"in_{n}": a for n, a in arrays.items()}

    nc = bacc.Bacc("TRN2", target_bir_lowering=False, num_devices=1)
    dram = {n: nc.dram_tensor(n, a.shape, mybir.dt.from_np(a.dtype), kind="ExternalInput").ap()
            for n, a in arrays.items()}
    out = nc.dram_tensor("out_rows", (TILES, P, D), F32, kind="ExternalOutput").ap()
    by_feature = [dram[f"in_b{n}"] for n in "qk"]
    on_all_rows = [dram[f"in_b{n}"].to_broadcast([P, D]) for n in "vo"]
    attention_kernel(nc, dram["in_xt"], dram["in_x"], dram["in_adj"], [dram[f"in_w{n}"] for n in "qkvo"],
                     by_feature + on_all_rows, out)
    result = run_bass_kernel_spmd(nc, [arrays], core_ids=[0])
    return result.results[0]["out_rows"].reshape(GRAPHS, NODES, D)
```

```python
from contextlib import ExitStack

import concourse.bass as bass
from concourse import mybir

F32 = mybir.dt.float32
F32R = mybir.dt.float32r
I32 = mybir.dt.int32
ALU = mybir.AluOpType
ACT = mybir.ActivationFunctionType
AX_X = mybir.AxisListType.X

P = 128
GRAPHS, NODES, D = 128, 64, 512
HEADS = 16
DH = D // HEADS
KC = D // P
HC = P // DH
SQ = 32
TILES = GRAPHS * NODES // P
GT = 4
GROUPS = TILES // GT
SCALE = float(DH) ** -0.5
EPS = 1e-5
MASKED = -3.0e38
DMA = 16
LOOP = 2 * GT
PEELED = 3
START = [("k", 0), ("q", 2), ("k", 1), ("q", 3), ("k", 2), ("k", 3)]
LAST = TILES - GT
UNITS = {LAST - 4: (0, 1), LAST - 3: (2,), LAST - 2: (3,), LAST - 1: (4, 5), LAST: (6,), LAST + 1: (7,)}
V_SHARED = LAST - GT + 1
WARM_START, WARM_PT, WARM_LAST_PT, WARM_LAST_OT = 9, 20, 12, 3


def wait_for(eng, sem, count):
    if not isinstance(count, int) or count > 0:
        eng.wait_ge(sem, count)


def attention_kernel(nc, xt_dram, x_dram, adj_dram, w_dram, b_dram, out_dram):
    ctx = ExitStack()
    with ctx:
        def sb(name, shape, dt=F32):
            return ctx.enter_context(nc.sbuf_tensor(name, shape, dt))

        def sem(name):
            return ctx.enter_context(nc.semaphore(name))

        w_hi = [sb(f"w{n}_hi", [P, KC, D], F32R) for n in "qkvo"]
        w_lo = [sb(f"w{n}_lo", [P, KC, D], F32R) for n in "qkvo"]
        x_raw = sb("x_raw", [P, 2, KC, D])
        x_hi = sb("x_hi", [P, 2, KC, D], F32R)
        x_lo = sb("x_lo", [P, 2, KC, D], F32R)
        qt = sb("qt", [P, 2, KC, D])
        kt = sb("kt", [P, 2, KC, D])
        kt_diag = sb("kt_diag", [P, KC, 2, HC, NODES])
        v = sb("v", [P, 2, D])
        row = sb("row", [P, 4, D])
        soft = sb("soft", [P, 2, HEADS * NODES])
        pt = sb("pt", [P, HEADS, P])
        ot_hi = sb("ot_hi", [P, KC, P], F32R)
        ot_lo = sb("ot_lo", [P, KC, P], F32R)
        adj = sb("adj", [P, GT, NODES], I32)
        bias = sb("bias", [P, 2, GT, NODES])
        bq = sb("bq", [P, KC])
        bk = sb("bk", [P, KC])
        bv = sb("bv", [P, D])
        bo = sb("bo", [P, D])
        top = sb("top", [P, 2, HEADS])
        total = sb("total", [P, 2, HEADS])
        inverse = sb("inverse", [P, 2, HEADS])
        stats = sb("stats", [P, 2, 6])
        moments = sb("moments", [P, 2, 2])
        shifted = sb("shifted", [P, 2, 1])
        rstd = sb("rstd", [P, 2, 1])
        eps = sb("eps", [P, 1])
        minus_half = sb("minus_half", [P, 1])

        psum_s = ctx.enter_context(nc.psum_tensor("psum_s", [P, 2, 2, D], F32))
        psum_ot = ctx.enter_context(nc.psum_tensor("psum_ot", [P, D], F32))
        psum_y = ctx.enter_context(nc.psum_tensor("psum_y", [P, D], F32))
        psum_v = ctx.enter_context(nc.psum_tensor("psum_v", [P, D], F32))
        psum_k = ctx.enter_context(nc.psum_tensor("psum_k", [P, D], F32))

        def y_bank(c):
            return {TILES - 2: psum_k, TILES - 1: psum_v}.get(c, psum_y)[:, :]

        wq_in = [sem(f"wq_in{n}") for n in range(KC)]
        wk_in = [sem(f"wk_in{n}") for n in range(KC)]
        x0_in = [sem(f"x0_in{n}") for n in range(KC)]
        w_in = {2: sem("wv_in"), 3: sem("wo_in")}
        b_in = sem("b_in")
        x_in = [sem("x_in0"), sem("x_in1")]
        adj_in = sem("adj_in")
        row_in = [sem(f"row_in{n}") for n in range(4)]
        stored = [sem(f"stored{n}") for n in range(4)]
        w_hi_done = sem("w_hi_done")
        w_lo_done = sem("w_lo_done")
        const_done, warm_done = sem("const_done"), sem("warm_done")
        x_hi_done = sem("x_hi_done")
        x_lo_done = sem("x_lo_done")
        q_proj, k_proj = sem("q_proj"), sem("k_proj")
        q_done, k_done = sem("q_done"), sem("k_done")
        bias_done = sem("bias_done")
        v_proj, v_done = sem("v_proj"), sem("v_done")
        v_copied = sem("v_copied")
        first_spread = sem("first_spread")
        spread_done = sem("spread_done")
        zeroed = sem("zeroed")
        scored = sem("scored")
        masked = sem("masked")
        topped = sem("topped")
        centred = sem("centred")
        exped = sem("exped")
        summed = sem("summed")
        inverted = sem("inverted")
        normed = sem("normed")
        squares_done = sem("squares_done")
        pt_done = sem("pt_done")
        mixed = sem("mixed")
        ot_hi_done = sem("ot_hi_done")
        ot_lo_done = sem("ot_lo_done")
        y_proj = sem("y_proj")
        row_biased = sem("row_biased")
        row_added = sem("row_added")
        row_stats = sem("row_stats")
        row_moments = sem("row_moments")
        row_shifted = sem("row_shifted")
        row_rstd = sem("row_rstd")
        row_done = sem("row_done")
        pe_went_on, dve_went_on, pool_went_on = sem("pe_went_on"), sem("dve_went_on"), sem("pool_went_on")

        w_raw = [qt[:, 1], kt[:, 1], row[:, :, :], soft[:, :, :].rearrange("p a (c n) -> p (a c) n", n=D)]

        def by_head(ap):
            return ap.rearrange("p (h k) -> p h k", k=NODES)

        def run_slots(eng, slot):
            for c in range(GT):
                slot(0, c)
            with eng.Fori(0, (GROUPS - 1 - PEELED) // 2) as i:
                for c in range(GT, GT + LOOP):
                    slot(i, c)
            for c in range(TILES - PEELED * GT, TILES + 3):
                slot(0, c)

        def norm(eng, ops, i, c):
            eng.wait_ge(inverted, 8 * i + c + 1)
            ops.tensor_tensor(by_head(soft[:, c % 2, :]), by_head(soft[:, c % 2, :]),
                              inverse[:, c % 2, :].unsqueeze(2).to_broadcast([P, HEADS, NODES]),
                              ALU.mult).then_inc(normed, 1)

        def spread(copy, c, r, chunks):
            f, t = slice(r * DH, (r + 1) * DH), c % GT
            return copy(kt_diag[f, chunks, :, r, :],
                        kt[f, c // GT % 2, chunks, t * P:(t + 1) * P].rearrange("p c (g k) -> p c g k", g=2))

        block = ctx.enter_context(nc.Block())

        @block.sync
        def _(sp):
            def load_x(i, c):
                g, buf = 2 * i + c // GT, c // GT % 2
                sp.dma_start(x_raw[:, buf], xt_dram[g]).then_inc(x_in[buf], DMA)

            def load_adj(i, c):
                sp.dma_start(adj[:, :, :], adj_dram[2 * i + c // GT]).then_inc(adj_in, DMA)

            def load_row(i, c):
                if c >= 4:
                    sp.wait_ge(stored[c % 4], DMA * (2 * i + c // 4))
                sp.dma_start(row[:, c % 4], x_dram[8 * i + c]).then_inc(row_in[c % 4], DMA)

            for kc in range(KC):
                sp.dma_start(w_raw[0][:, kc, :], w_dram[0][:, kc, :]).then_inc(wq_in[kc], DMA)
                sp.dma_start(x_raw[:, 0, kc, :], xt_dram[0, :, kc, :]).then_inc(x0_in[kc], DMA)
            for kc in range(KC):
                sp.dma_start(w_raw[1][:, kc, :], w_dram[1][:, kc, :]).then_inc(wk_in[kc], DMA)
            for dst, src in zip((bq, bk, bv, bo), b_dram):
                sp.dma_start(dst[:, :], src).then_inc(b_in, DMA)
            sp.dma_start(w_raw[2], w_dram[2]).then_inc(w_in[2], DMA)
            load_adj(0, 0)
            load_x(0, GT)
            sp.dma_start(w_raw[3], w_dram[3]).then_inc(w_in[3], DMA)
            sp.wait_ge(x_hi_done, KC)
            sp.wait_ge(x_lo_done, KC)
            load_x(0, 2 * GT)
            sp.wait_ge(w_hi_done, 3 * KC)
            sp.wait_ge(w_lo_done, 3 * KC)

            def slot(i, c):
                T = 8 * i + c
                if c % GT == 0 and c < TILES - GT:
                    sp.wait_ge(bias_done, 2 * i + c // GT + 1)
                    load_adj(i, c + GT)
                if c % GT == 0 and c < TILES - 3 * GT:
                    sp.wait_ge(x_hi_done, T + 2 * GT)
                    sp.wait_ge(x_lo_done, T + 2 * GT)
                    load_x(i, c + 3 * GT)
                if c < TILES:
                    load_row(i, c)
                if c >= 3:
                    sp.wait_ge(row_done, T - 2)
                    sp.dma_start(out_dram[T - 3], row[:, (c - 3) % 4]).then_inc(stored[(c - 3) % 4], DMA)

            run_slots(sp, slot)
            for n in range(4):
                sp.wait_ge(stored[n], DMA * TILES // 4)

        @block.tensor
        def _(pe):
            def split_matmul(out, kc, left_hi, left_lo, right_hi, right_lo):
                nc.tensor.matmul(out, left_hi, right_hi, start=kc == 0, stop=False)
                nc.tensor.matmul(out, left_hi, right_lo, start=False, stop=False)
                return nc.tensor.matmul(out, left_lo, right_hi, start=False, stop=kc == KC - 1)

            def project_v(i, c, kc):
                T, buf, at = 8 * i + c, c // GT % 2, slice(c % GT * P, (c % GT + 1) * P)
                if kc == 0:
                    if c == 0:
                        pe.wait_ge(w_hi_done, 3 * KC)
                        pe.wait_ge(w_lo_done, 3 * KC)
                    if c <= LAST - GT:
                        pe.wait_ge(q_done, T + GT)
                    elif len(UNITS.get(c - 1, ())) > 1:
                        pe.wait_ge(q_done, LAST + UNITS[c - 1][1] // 2 + 1)
                    else:
                        pe.wait_ge(v_done, T)
                last = split_matmul(psum_v[:, :], kc, x_hi[:, buf, kc, at], x_lo[:, buf, kc, at],
                                    w_hi[2][:, kc, :], w_lo[2][:, kc, :])
                if kc == KC - 1:
                    last.then_inc(v_proj, 1)

            def project_q_chunk(i, c, kc, bank):
                buf, m = c // GT % 2, slice(c % GT * P, (c % GT + 1) * P)
                return split_matmul(bank, kc, w_hi[0][:, kc, m], w_lo[0][:, kc, m],
                                    x_hi[:, buf, kc, :], x_lo[:, buf, kc, :])

            def project_q(i, c):
                if c < GT:
                    pe.wait_ge(q_done, c)
                else:
                    pe.wait_ge(v_done, 8 * i + c - GT + 1)
                for kc in range(KC):
                    last = project_q_chunk(i, c, kc, psum_v[:, :])
                last.then_inc(q_proj, 1)

            def project_k(i, c, bank=psum_k[:, :]):
                J, buf, m = 8 * i + c, c // GT % 2, slice(c % GT * P, (c % GT + 1) * P)
                if c != 3:
                    wait_for(pe, k_done, J)
                if c % GT == 0 and c > 0:
                    pe.wait_ge(x_hi_done, J + GT)
                    pe.wait_ge(x_lo_done, J + GT)
                for kc in range(KC):
                    if c == 0:
                        pe.wait_ge(w_hi_done, KC + kc + 1)
                        pe.wait_ge(w_lo_done, KC + kc + 1)
                    last = split_matmul(bank, kc, w_hi[1][:, kc, m], w_lo[1][:, kc, m],
                                        x_hi[:, buf, kc, :], x_lo[:, buf, kc, :])
                last.then_inc(k_proj, 1)

            def project_unit(n, bank):
                buf, half, w, proj = LAST // GT % 2, n // 4 * 2 * P, 1 - n % 2, (k_proj, q_proj)[n % 2]
                if n == 0:
                    pe.wait_ge(x_hi_done, TILES)
                    pe.wait_ge(x_lo_done, TILES)
                for m in (n // 2 % 2 * 2, n // 2 % 2 * 2 + 1):
                    for kc in range(KC):
                        last = split_matmul(bank[:, m % 2 * 2 * P:(m % 2 + 1) * 2 * P], kc,
                                            w_hi[w][:, kc, m * P:(m + 1) * P], w_lo[w][:, kc, m * P:(m + 1) * P],
                                            x_hi[:, buf, kc, half:half + 2 * P], x_lo[:, buf, kc, half:half + 2 * P])
                last.then_inc(proj, 1)

            def score(i, c, kc):
                T, buf, t = 8 * i + c, c // GT % 2, c % GT
                if t == 0 and c < LAST:
                    pe.wait_ge(q_done, T + kc + 1)
                elif t % 2 == 0 and c >= LAST:
                    pe.wait_ge(q_done, LAST + t + kc // 2 + 1)
                if c == 0:
                    pe.wait_ge(first_spread, kc + 1)
                elif kc == 0:
                    pe.wait_ge(spread_done, T)
                if kc == 0:
                    wait_for(pe, masked, T - 1)
                for graph in range(2):
                    rows = slice(t * P + graph * NODES, t * P + (graph + 1) * NODES)
                    last = nc.tensor.matmul(
                        psum_s[graph * NODES:(graph + 1) * NODES, c % 2, kc // 2,
                               kc % 2 * HC * NODES:(kc % 2 + 1) * HC * NODES],
                        qt[:, buf, kc, rows], kt_diag[:, kc, graph, :, :].rearrange("p h k -> p (h k)"),
                        start=True, stop=True)
                if kc == KC - 1:
                    last.then_inc(scored, 1)

            def mix(i, c):
                T = 8 * i + c
                pe.wait_ge(pt_done, T + 1)
                pe.wait_ge(v_done, T + 1)
                pe.sem_inc(pe_went_on, 1)
                for h in range(HEADS):
                    r, kc = h % HC, h // HC
                    last = nc.tensor.matmul(psum_ot[r * DH:(r + 1) * DH, kc * P:(kc + 1) * P],
                                            v[:, c % 2, h * DH:(h + 1) * DH], pt[:, h, :],
                                            start=True, stop=True)
                last.then_inc(mixed, 1)

            def project_out(i, c):
                T = 8 * i + c
                pe.wait_ge(ot_hi_done, T + 1)
                if c == TILES - 2:
                    pe.wait_ge(q_done, TILES)
                elif c == TILES - 1:
                    pe.wait_ge(v_copied, TILES - V_SHARED)
                else:
                    wait_for(pe, row_added, T)
                if c == 0:
                    pe.wait_ge(w_hi_done, 4 * KC)
                    pe.wait_ge(w_lo_done, 4 * KC)
                for kc in range(KC):
                    nc.tensor.matmul(y_bank(c), ot_hi[:, kc, :], w_hi[3][:, kc, :], start=kc == 0, stop=False)
                    nc.tensor.matmul(y_bank(c), ot_hi[:, kc, :], w_lo[3][:, kc, :], start=False, stop=False)
                pe.wait_ge(ot_lo_done, T + 1)
                for kc in range(KC):
                    last = nc.tensor.matmul(y_bank(c), ot_lo[:, kc, :], w_hi[3][:, kc, :],
                                            start=False, stop=kc == KC - 1)
                last.then_inc(y_proj, 1)

            def slot(i, c):
                if c < TILES:
                    for kc in range(KC):
                        score(i, c, kc)
                    if c == TILES - 1:
                        mix(0, c - 2)
                    for kc in range(KC):
                        project_v(i, c, kc)
                if 2 <= c <= TILES + 1:
                    project_out(i, c - 2)
                if c < LAST - GT:
                    project_k(i, c + GT)
                    project_q(i, c + GT)
                elif c in UNITS:
                    n = UNITS[c][0]
                    pe.wait_ge((q_done, k_done)[n % 2], LAST + (n + 1) // 2)
                    project_unit(n, psum_k)
                    if len(UNITS[c]) > 1:
                        pe.wait_ge(v_done, c + 1)
                        project_unit(UNITS[c][1], psum_v)
                if c in (TILES - 1, TILES):
                    pe.wait_ge(v_copied, TILES - V_SHARED)
                    keep_warm(WARM_PT if c < TILES else WARM_LAST_PT)
                if 1 <= c <= TILES and c != TILES - 2:
                    mix(i, c - 1)
                if c == TILES:
                    keep_warm(WARM_LAST_OT)

            def keep_warm(count):
                for _ in range(count):
                    nc.tensor.matmul(psum_v[:, :], w_hi[3][:, 0, 0:P], w_hi[3][:, 0, :], start=True, stop=True)

            pe.wait_ge(warm_done, 1)
            keep_warm(WARM_START)
            for kc in range(KC):
                pe.wait_ge(w_hi_done, kc + 1)
                pe.wait_ge(w_lo_done, kc + 1)
                pe.wait_ge(x_hi_done, kc + 1)
                pe.wait_ge(x_lo_done, kc + 1)
                first = project_q_chunk(0, 0, kc, psum_v[:, :])
                second = project_q_chunk(0, 1, kc, psum_ot[:, :])
            first.then_inc(q_proj, 1)
            second.then_inc(q_proj, 1)
            for project, c in START:
                if project == "q":
                    project_q(0, c)
                elif c < 3:
                    project_k(0, c)
                else:
                    project_k(0, c, psum_ot[:, :])
            run_slots(pe, slot)

        @block.scalar
        def _(act):
            def split_x(i, c):
                buf, t = c // GT % 2, c % GT
                if t == 0:
                    act.wait_ge(x_in[buf], DMA * (i + c // GT // 2 + (1 if buf else 0)))
                    if c >= 2 * GT:
                        act.wait_ge(q_proj, 8 * i + c - GT)
                if c >= 2 * GT:
                    act.wait_ge(v_proj, 8 * i + c - 2 * GT + 1)
                rows = slice(t * P, (t + 1) * P)
                nc.scalar.copy(x_hi[:, buf, :, rows], x_raw[:, buf, :, rows]).then_inc(x_hi_done, 1)

            def read_q(i, c, bank=psum_v[:, :]):
                J, buf, m = 8 * i + c, c // GT % 2, c % GT
                act.wait_ge(q_proj, J + 1)
                if c >= 2 * GT:
                    act.wait_ge(scored, J - m - GT)
                nc.scalar.activation(qt[:, buf, m, :], bank, ACT.Identity,
                                     bias=bq[:, m:m + 1], scale=1.0).then_inc(q_done, 1)

            def read_k(i, c, bank=psum_k[:, :]):
                J, buf, m = 8 * i + c, c // GT % 2, c % GT
                act.wait_ge(k_proj, J + 1)
                if c >= 2 * GT:
                    act.wait_ge(scored, J - m - GT)
                nc.scalar.activation(kt[:, buf, m, :], bank, ACT.Identity,
                                     bias=bk[:, m:m + 1], scale=1.0).then_inc(k_done, 1)

            def read_unit(n, bank):
                buf, half = LAST // GT % 2, n // 4 * 2 * P
                to, b, proj, done = ((kt, bk, k_proj, k_done), (qt, bq, q_proj, q_done))[n % 2]
                act.wait_ge(proj, LAST + n // 2 + 1)
                act.wait_ge(scored, LAST - GT)
                for m in (n // 2 % 2 * 2, n // 2 % 2 * 2 + 1):
                    last = nc.scalar.activation(
                        to[:, buf, m, half:half + 2 * P], bank[:, m % 2 * 2 * P:(m % 2 + 1) * 2 * P],
                        ACT.Identity, bias=b[:, m:m + 1], scale=1.0)
                last.then_inc(done, 1)

            def copy_v(c):
                act.wait_ge(v_proj, c + 1)
                act.wait_ge(mixed, c - 1)
                nc.scalar.copy(v[:, c % 2, :], psum_v[:, :]).then_inc(v_copied, 1)

            def exp(i, c):
                T = 8 * i + c
                act.wait_ge(centred, T + 1)
                nc.scalar.activation(soft[:, c % 2, :], soft[:, c % 2, :], ACT.Exp,
                                     scale=SCALE).then_inc(exped, 1)

            def spread_k(i, c):
                T = 8 * i + c
                act.wait_ge(scored, T)
                if c >= LAST:
                    if c % 2 == 0:
                        act.wait_ge(k_done, LAST + c % GT + 2)
                elif c % GT == 0:
                    act.wait_ge(k_done, T + GT)
                for r in range(HC):
                    last = spread(nc.scalar.copy, c, r, slice(0, KC))
                last.then_inc(spread_done, 1)

            def read_ot(i, c):
                T = 8 * i + c
                act.wait_ge(mixed, T + 1)
                wait_for(act, y_proj, T)
                nc.scalar.copy(ot_hi[:, :, :].rearrange("p c q -> p (c q)"), psum_ot[:, :]).then_inc(ot_hi_done, 1)

            def slot(i, c):
                early = (c + 1) % GT != 0 or c >= LAST - GT
                if c < TILES - 1 and early:
                    spread_k(i, c + 1)
                if c < TILES - 2 * GT:
                    split_x(i, c + 2 * GT)
                if V_SHARED <= c < TILES:
                    copy_v(c)
                if c < TILES:
                    exp(i, c)
                if c < LAST - GT:
                    read_k(i, c + GT)
                elif c in UNITS:
                    read_unit(UNITS[c][0], psum_k)
                if c < TILES - 1 and not early:
                    spread_k(i, c + 1)
                if c < LAST - GT:
                    read_q(i, c + GT)
                elif len(UNITS.get(c, ())) > 1:
                    read_unit(UNITS[c][1], psum_v)
                if 1 <= c <= TILES:
                    read_ot(i, c - 1)

            def split_w(n, kc):
                if n == 0:
                    act.wait_ge(wq_in[kc], DMA)
                elif n == 1:
                    act.wait_ge(wk_in[kc], DMA)
                elif kc == 0:
                    act.wait_ge(w_in[n], DMA)
                nc.scalar.copy(w_hi[n][:, kc, :], w_raw[n][:, kc, :]).then_inc(w_hi_done, 1)

            for kc in range(KC):
                split_w(0, kc)
                act.wait_ge(x0_in[kc], DMA)
                nc.scalar.copy(x_hi[:, 0, kc, :], x_raw[:, 0, kc, :]).then_inc(x_hi_done, 1)
            for kc in range(KC):
                split_w(1, kc)
            act.wait_ge(b_in, DMA * 4)
            read_q(0, 0)
            read_q(0, 1, psum_ot[:, :])
            for n, (project, c) in enumerate(START):
                if project == "q":
                    read_q(0, c)
                elif c < 3:
                    read_k(0, c)
                else:
                    read_k(0, c, psum_ot[:, :])
                for part in (n % 2 * 2, n % 2 * 2 + 1):
                    if n < 2:
                        split_w(2, part)
                    elif n < 4:
                        split_x(0, GT + part)
                    else:
                        split_w(3, part)
            run_slots(act, slot)

        @block.vector
        def _(dve):
            def split_x(i, c):
                buf, rows = c // GT % 2, slice(c % GT * P, (c % GT + 1) * P)
                dve.wait_ge(x_hi_done, 8 * i + c + 1)
                nc.vector.tensor_tensor(x_lo[:, buf, :, rows], x_raw[:, buf, :, rows],
                                        x_hi[:, buf, :, rows].bitcast(F32), ALU.subtract).then_inc(x_lo_done, 1)

            def read_v(i, c):
                T = 8 * i + c
                dve.wait_ge(v_proj, T + 1)
                wait_for(dve, mixed, T - 1)
                nc.vector.tensor_tensor(v[:, c % 2, :], psum_v[:, :], bv[:, :], ALU.add).then_inc(v_done, 1)

            def mask(i, c):
                T = 8 * i + c
                if c % GT == 0:
                    dve.wait_ge(bias_done, 2 * i + c // GT + 1)
                dve.wait_ge(scored, T + 1)
                wait_for(dve, pt_done, T - 1)
                nc.vector.tensor_tensor(
                    by_head(soft[:, c % 2, :]),
                    psum_s[:, c % 2].rearrange("p b (h k) -> p (b h) k", k=NODES),
                    bias[:, c // GT % 2, c % GT, :].unsqueeze(1).to_broadcast([P, HEADS, NODES]),
                    ALU.add).then_inc(masked, 1)
                dve.wait_ge(masked, T + 1)
                nc.vector.tensor_reduce(top[:, c % 2, :], by_head(soft[:, c % 2, :]), AX_X,
                                        ALU.max).then_inc(topped, 1)

            def transpose(i, c):
                T = 8 * i + c
                dve.wait_ge(normed, T + 1)
                wait_for(dve, mixed, T)
                for graph in range(2):
                    own = slice(graph * NODES, (graph + 1) * NODES)
                    last = nc.vector.transpose(pt[own, :, own], by_head(soft[own, c % 2, :]))
                last.then_inc(squares_done, 1)
                dve.wait_ge(squares_done, T + 1)
                for q0 in range(0, P, SQ):
                    half = q0 // SQ % 2
                    k0 = q0 + SQ * (1 - 2 * half)
                    keys = slice((1 - half) * SQ, (2 - half) * SQ)
                    last = nc.vector.transpose(pt[k0:k0 + SQ, :, q0:q0 + SQ],
                                               by_head(soft[q0:q0 + SQ, c % 2, :])[:, :, keys])
                last.then_inc(pt_done, 1)

            def sum_up(i, c):
                T = 8 * i + c
                dve.wait_ge(exped, T + 1)
                nc.vector.tensor_reduce(total[:, c % 2, :], by_head(soft[:, c % 2, :]), AX_X,
                                        ALU.add).then_inc(summed, 1)
                dve.wait_ge(summed, T + 1)
                nc.vector.reciprocal(inverse[:, c % 2, :], total[:, c % 2, :]).then_inc(inverted, 1)

            def split_ot(i, c):
                T = 8 * i + c
                dve.wait_ge(ot_hi_done, T + 1)
                wait_for(dve, y_proj, T)
                nc.vector.tensor_tensor(ot_lo[:, :, :].rearrange("p c q -> p (c q)"), psum_ot[:, :],
                                        ot_hi[:, :, :].rearrange("p c q -> p (c q)").bitcast(F32),
                                        ALU.subtract).then_inc(ot_lo_done, 1)

            def add_row(i, c):
                T = 8 * i + c
                dve.wait_ge(y_proj, T + 1)
                dve.wait_ge(row_biased, T + 1)
                nc.vector.tensor_tensor(row[:, c % 4, :], y_bank(c), row[:, c % 4, :],
                                        ALU.add).then_inc(row_added, 1)
                dve.wait_ge(row_added, T + 1)
                nc.vector.bn_stats(stats[:, c % 2, :], row[:, c % 4, :]).then_inc(row_stats, 1)
                dve.wait_ge(row_stats, T + 1)
                dve.sem_inc(dve_went_on, 1)
                nc.vector.bn_aggr(moments[:, c % 2, :], stats[:, c % 2, :]).then_inc(row_moments, 1)

            def norm_row(i, c):
                T = 8 * i + c
                dve.wait_ge(row_rstd, T + 1)
                nc.vector.tensor_scalar(row[:, c % 4, :], row[:, c % 4, :], moments[:, c % 2, 0:1],
                                        rstd[:, c % 2, :], ALU.subtract, ALU.mult).then_inc(row_done, 1)

            def slot(i, c):
                if c < TILES:
                    mask(i, c)
                if c < V_SHARED:
                    read_v(i, c)
                if 1 <= c < TILES:
                    transpose(i, c - 1)
                if c < TILES:
                    sum_up(i, c)
                if c < TILES - 1:
                    if c >= 3:
                        norm_row(i, c - 3)
                    if c >= 2:
                        add_row(i, c - 2)
                    if c >= 1:
                        split_ot(i, c - 1)
                elif c == TILES - 1:
                    norm(dve, nc.vector, 0, c)
                    split_ot(0, c - 1)
                    transpose(0, c)
                    norm_row(0, c - 3)
                    add_row(0, c - 2)
                elif c == TILES:
                    split_ot(0, c - 1)
                    add_row(0, c - 2)
                    norm_row(0, c - 3)
                elif c == TILES + 1:
                    add_row(0, c - 2)
                    norm_row(0, c - 3)
                else:
                    norm_row(0, c - 3)

            def split_w(n, kc):
                dve.wait_ge(w_hi_done, n * KC + kc + 1)
                nc.vector.tensor_tensor(w_lo[n][:, kc, :], w_raw[n][:, kc, :],
                                        w_hi[n][:, kc, :].bitcast(F32), ALU.subtract).then_inc(w_lo_done, 1)

            nc.vector.memset(w_hi[3][:, 0, :].bitcast(F32), 0.0).then_inc(warm_done, 1)
            for kc in range(KC):
                split_w(0, kc)
                dve.wait_ge(x_hi_done, kc + 1)
                nc.vector.tensor_tensor(x_lo[:, 0, kc, :], x_raw[:, 0, kc, :],
                                        x_hi[:, 0, kc, :].bitcast(F32), ALU.subtract).then_inc(x_lo_done, 1)

            def spread_first(kc):
                dve.wait_ge(k_done, kc + 1)
                for r in range(HC):
                    last = spread(nc.vector.tensor_copy, 0, r, slice(kc, kc + 1))
                last.then_inc(first_spread, 1)

            for kc in range(KC):
                split_w(1, kc)
            dve.wait_ge(zeroed, 1)
            spread_first(0)
            for kc in range(KC):
                split_w(2, kc)
            spread_first(1)
            dve.wait_ge(b_in, DMA * 4)
            for c in range(GT, 2 * GT):
                split_x(0, c)
            for half in range(2):
                spread_first(2 + half)
                split_w(3, 2 * half)
                split_w(3, 2 * half + 1)
            dve.wait_ge(w_lo_done, 4 * KC)
            run_slots(dve, slot)

        @block.gpsimd
        def _(pool):
            def split_x(i, c):
                buf, rows = c // GT % 2, slice(c % GT * P, (c % GT + 1) * P)
                if c == 2 * GT:
                    pool.wait_ge(x_lo_done, c)
                pool.wait_ge(x_hi_done, 8 * i + c + 1)
                nc.gpsimd.tensor_tensor(x_lo[:, buf, :, rows], x_raw[:, buf, :, rows],
                                        x_hi[:, buf, :, rows].bitcast(F32), ALU.subtract).then_inc(x_lo_done, 1)

            def add_bv(c):
                pool.wait_ge(v_copied, c - V_SHARED + 1)
                nc.gpsimd.tensor_tensor(v[:, c % 2, :], v[:, c % 2, :], bv[:, :], ALU.add).then_inc(v_done, 1)

            def make_bias(i, c):
                g, buf = 2 * i + c // GT, c // GT % 2
                pool.wait_ge(adj_in, DMA * (g + 1))
                if c >= 2 * GT:
                    pool.wait_ge(masked, 4 * g - GT)
                pool.sem_inc(pool_went_on, 1)
                nc.gpsimd.tensor_scalar(bias[:, buf], adj[:, :, :], 0.0, MASKED, ALU.is_equal,
                                        ALU.mult).then_inc(bias_done, 1)

            def add_bo(i, c):
                T = 8 * i + c
                pool.wait_ge(row_in[c % 4], DMA * (2 * i + c // 4 + 1))
                nc.gpsimd.tensor_tensor(row[:, c % 4, :], row[:, c % 4, :], bo[:, :],
                                        ALU.add).then_inc(row_biased, 1)

            def centre(i, c):
                pool.wait_ge(topped, 8 * i + c + 1)
                nc.gpsimd.tensor_tensor(by_head(soft[:, c % 2, :]), by_head(soft[:, c % 2, :]),
                                        top[:, c % 2, :].unsqueeze(2).to_broadcast([P, HEADS, NODES]),
                                        ALU.subtract).then_inc(centred, 1)

            def make_rstd(i, c):
                T = 8 * i + c
                pool.wait_ge(row_moments, T + 1)
                nc.gpsimd.tensor_tensor(shifted[:, c % 2, :], moments[:, c % 2, 1:2], eps[:, :],
                                        ALU.add).then_inc(row_shifted, 1)
                pool.wait_ge(row_shifted, T + 1)
                nc.gpsimd.tensor_tensor(rstd[:, c % 2, :], shifted[:, c % 2, :], minus_half[:, :],
                                        ALU.pow).then_inc(row_rstd, 1)

            def slot(i, c):
                if c < TILES:
                    centre(i, c)
                if V_SHARED <= c < TILES:
                    add_bv(c)
                if c < TILES - 2 * GT:
                    split_x(i, c + 2 * GT)
                if c % GT == 1 and c < TILES - GT:
                    make_bias(i, c + GT)
                if c < TILES - 1:
                    norm(pool, nc.gpsimd, i, c)
                if 2 <= c <= TILES + 1:
                    make_rstd(i, c - 2)
                if c < TILES:
                    add_bo(i, c)

            nc.gpsimd.memset(pt[:, :, :], 0.0)
            nc.gpsimd.memset(kt_diag[:, :, :, :, :], 0.0).then_inc(zeroed, 1)
            nc.gpsimd.memset(eps[:, :], EPS)
            nc.gpsimd.memset(minus_half[:, :], -0.5).then_inc(const_done, 1)
            pool.wait_ge(const_done, 1)
            make_bias(0, 0)
            pool.wait_ge(b_in, DMA * 4)
            run_slots(pool, slot)


def kernel(x, adj, L0_gnn_Wq, L0_gnn_bq, L0_gnn_Wk, L0_gnn_bk, L0_gnn_Wv, L0_gnn_bv, L0_gnn_Wo, L0_gnn_bo):
    import numpy as np
    import concourse.bacc as bacc
    from concourse.bass_utils import run_bass_kernel_spmd

    x, adj = np.asarray(x), np.asarray(adj)
    rows = x.reshape(TILES, P, D)
    arrays = {
        "xt": np.ascontiguousarray(x.reshape(GROUPS, GT * P, KC, P).transpose(0, 3, 2, 1)),
        "x": np.ascontiguousarray(rows),
        "adj": np.ascontiguousarray(adj.reshape(GROUPS, GT, P, NODES).transpose(0, 2, 1, 3)),
    }
    for name, w in zip("qkvo", (L0_gnn_Wq, L0_gnn_Wk, L0_gnn_Wv, L0_gnn_Wo)):
        arrays["w" + name] = np.ascontiguousarray(np.asarray(w).reshape(KC, P, D).transpose(1, 0, 2))
    for name, b in zip("qkvo", (L0_gnn_bq, L0_gnn_bk, L0_gnn_bv, L0_gnn_bo)):
        b = np.asarray(b)
        arrays["b" + name] = np.ascontiguousarray(b.reshape(KC, P).T if name in "qk" else b.reshape(1, D))
    arrays = {f"in_{n}": a for n, a in arrays.items()}

    nc = bacc.Bacc("TRN2", target_bir_lowering=False, num_devices=1)
    dram = {n: nc.dram_tensor(n, a.shape, mybir.dt.from_np(a.dtype), kind="ExternalInput").ap()
            for n, a in arrays.items()}
    out = nc.dram_tensor("out_rows", (TILES, P, D), F32, kind="ExternalOutput").ap()
    by_feature = [dram[f"in_b{n}"] for n in "qk"]
    on_all_rows = [dram[f"in_b{n}"].to_broadcast([P, D]) for n in "vo"]
    attention_kernel(nc, dram["in_xt"], dram["in_x"], dram["in_adj"], [dram[f"in_w{n}"] for n in "qkvo"],
                     by_feature + on_all_rows, out)
    result = run_bass_kernel_spmd(nc, [arrays], core_ids=[0])
    return result.results[0]["out_rows"].reshape(GRAPHS, NODES, D)
```
